# Optimizing a Trainium2 kernel written in Bass

```python
import numpy as np
import jax
import jax.numpy as jnp

def _softmax(x, axis=-1):
    return jax.nn.softmax(x, axis=axis)

def _gelu(x):
    return jax.nn.gelu(x, approximate=True)

def _silu(x):
    return jax.nn.silu(x)

def _sigmoid(x):
    return jax.nn.sigmoid(x)

def _layernorm(x, axis=-1, eps=1e-05):
    m = jnp.mean(x, axis=axis, keepdims=True)
    v = jnp.var(x, axis=axis, keepdims=True)
    return (x - m) / jnp.sqrt(v + eps)

def _scatter_add(tgt, idx, src, axis=0):
    return tgt.at[idx].add(src)

def _segment_sum(src, seg, n):
    return jax.ops.segment_sum(src, seg, n)
kernel_name = 'mk_gnn_resnorm_d1_gnn_r32_aa9f8e'

def setup_inputs(seed: int=0):
    np.random.seed(seed)
    _w = jnp.asarray

    def _rec_inputs():
        import jax
        import jax.numpy as jnp
        _gk = jax.random.key(seed)
        x = -0.0001394 + 0.9999 * jax.random.normal(jax.random.fold_in(_gk, 1), (50000, 768), jnp.float32)
        src = jax.random.randint(jax.random.fold_in(_gk, 2), (25000,), 0, 50000, jnp.int32)
        dst = jnp.minimum((50000 * jax.random.uniform(jax.random.fold_in(_gk, 3), (25000,)) ** 2.0).astype(jnp.int32), 49999)
        _o = jnp.argsort(dst, stable=True)
        src = src[_o]
        dst = dst[_o]
        return (x, src, dst)
    x, src, dst = _rec_inputs()

    def _L0_gnn_setup():
        import jax, jax.numpy as jnp
        import numpy as np
        N = 50000
        E = 250000
        H = 12
        D = 64
        NEG_SLOPE = 0.2
        key = jax.random.key(seed)
        k1, k2, k3, k4, k5, k6, k7 = jax.random.split(key, 7)
        h = jax.random.normal(k1, (N, H * D), dtype=jnp.float32)
        src = jnp.concatenate([jnp.arange(N, dtype=jnp.int32), jax.random.randint(k2, (E - N,), 0, N, dtype=jnp.int32)])
        dst = jnp.concatenate([jnp.arange(N, dtype=jnp.int32), jax.random.randint(k3, (E - N,), 0, N, dtype=jnp.int32)])
        xav = 1.414 / np.sqrt(D)
        W_fc = jax.random.normal(k4, (D, D), dtype=jnp.float32) * xav
        attn_l = jax.random.normal(k5, (H, D), dtype=jnp.float32) * 0.15
        attn_r = jax.random.normal(k6, (H, D), dtype=jnp.float32) * 0.15
        W_res = jax.random.normal(k7, (D, D), dtype=jnp.float32) * xav
        return {'h': h, 'W_fc': W_fc, 'attn_l': attn_l, 'attn_r': attn_r, 'W_res': W_res, 'src': src, 'dst': dst}
    _L0_gnn_all = _L0_gnn_setup()
    _L0_gnn_in = {k: v for k, v in _L0_gnn_all.items() if k in ('W_fc', 'attn_l', 'attn_r', 'W_res')}
    del _L0_gnn_all
    return {'x': x, 'src': src, 'dst': dst, 'L0_gnn_W_fc': _L0_gnn_in['W_fc'], 'L0_gnn_attn_l': _L0_gnn_in['attn_l'], 'L0_gnn_attn_r': _L0_gnn_in['attn_r'], 'L0_gnn_W_res': _L0_gnn_in['W_res']}

def reference(x, src, dst, L0_gnn_W_fc, L0_gnn_attn_l, L0_gnn_attn_r, L0_gnn_W_res):
    import jax
    import jax.numpy as jnp

    def _L0_gnn_ref(h, W_fc, attn_l, attn_r, W_res, src, dst):
        import jax, jax.numpy as jnp
        import numpy as np
        N = 50000
        E = 250000
        H = 12
        D = 64
        NEG_SLOPE = 0.2
        n = h.shape[0]
        hh = h.reshape(n, H, D)
        ft = jnp.einsum('nhd,ed->nhe', hh, W_fc)
        a1 = jnp.einsum('nhd,hd->nh', ft, attn_l)
        a2 = jnp.einsum('nhd,hd->nh', ft, attn_r)
        e = jax.nn.leaky_relu(a1[src] + a2[dst], negative_slope=NEG_SLOPE)
        m = jax.ops.segment_max(e, dst, num_segments=n)
        ee = jnp.exp(e - m[dst])
        denom = jax.ops.segment_sum(ee, dst, num_segments=n)
        alpha = ee / denom[dst]
        agg = jax.ops.segment_sum(alpha[:, :, None] * ft[src], dst, num_segments=n)
        res = jnp.einsum('nhd,ed->nhe', hh, W_res)
        return jax.nn.relu((res + agg).reshape(n, H * D))
    x = _layernorm(x + _L0_gnn_ref(x, L0_gnn_W_fc, L0_gnn_attn_l, L0_gnn_attn_r, L0_gnn_W_res, src, dst), axis=-1)
    return x

_drawn_inputs = setup_inputs


def setup_inputs(seed=0):
    import zlib

    import numpy as np

    out = dict(_drawn_inputs(seed))
    spreads = {}
    factors = {}
    for name, (base, spread) in spreads.items():
        noise = np.random.default_rng([zlib.crc32(name.encode()), seed]).standard_normal(out[name].shape)
        drawn = base * np.exp(spread * noise) if base else spread * noise
        out[name] = jnp.asarray(drawn.astype(out[name].dtype))
    for name, factor in factors.items():
        out[name] = (out[name] * factor).astype(out[name].dtype)
    return out
```

```python
from contextlib import ExitStack

import concourse.bass as bass
from concourse import mybir

H, D = 12, 64
F = H * D
P = 128
C = F // P
PAIR = 2 * D + 4
EB = P - 1
EPS = 1e-5
SLOPE = 0.2
BIG = 1 << 20
APART = 1.0e33
LOWEST = -2.0e38


def gnn_program(nc, x, W_fc, attn_l, attn_r, W_res, cols, rows, out):
    fp32, i32 = mybir.dt.float32, mybir.dt.int32
    ALU, ACT = mybir.AluOpType, mybir.ActivationFunctionType
    N = x.shape[0]
    NBLK = cols.shape[1]
    G = 2 * P
    NG = -(-N // G)
    LAST0 = N - G
    FRESH = (NG - 1) * G - LAST0
    S = 4

    table = nc.dram_tensor("attention_terms", [N, 4 * C], fp32).ap()

    ctx = ExitStack()
    with ctx:
        def sb(name, shape, dt=fp32):
            return ctx.enter_context(nc.sbuf_tensor(name, shape, dt))

        def sem(name):
            return ctx.enter_context(nc.semaphore(name))

        def wait(eng, s, value):
            if not (isinstance(value, int) and value <= 0):
                eng.wait_ge(s, value)

        def hold(eng, s, value):
            if not (isinstance(value, int) and value <= 0):
                eng.wait_ge(s, value)
                eng.sem_inc(held, 1)

        psum = ctx.enter_context(nc.psum_tensor("psum", [P, 8 * 512], fp32))
        ident = sb("ident", [P, P])
        wtmp = sb("wtmp", [D, 3, D])
        attn_rows = sb("attn_rows", [H, 2, D])
        attn_cols = sb("attn_cols", [D, 2, H])
        w_node = sb("w_node", [P, C, PAIR])
        w_agg = sb("w_agg", [P, P])
        half = sb("half", [P, 1])
        zero1 = sb("zero1", [P, 1])

        held = sem("held")
        s_const, s_w, s_attn = sem("s_const"), sem("s_w"), sem("s_attn")
        s_attn_t, s_attn_c, s_wt, s_wset, s_u, s_uc = (sem(n) for n in
            ("s_attn_t", "s_attn_c", "s_wt", "s_wset", "s_u", "s_uc"))
        with nc.Block() as block:
            @block.sync
            def _(sp):
                for m, w in enumerate((W_fc, W_res, W_fc)):
                    sp.dma_start(wtmp[:, m, :], w).then_inc(s_w, 16)
                for m, a in enumerate((attn_l, attn_r)):
                    sp.dma_start(attn_rows[:, m, :], a).then_inc(s_attn, 16)

            @block.gpsimd
            def _(pool):
                nc.gpsimd.memset(ident[:], 0.0).then_inc(s_const, 1)
                nc.gpsimd.memset(half[:], -0.5).then_inc(s_const, 1)
                nc.gpsimd.memset(zero1[:], 0.0).then_inc(s_const, 1)
                nc.gpsimd.memset(w_node[:], 0.0).then_inc(s_const, 1)
                nc.gpsimd.memset(w_agg[:], 0.0).then_inc(s_const, 1)
                pool.wait_ge(s_const, 5)
                nc.gpsimd.affine_select(out=ident[:], in_=ident[:], compare_op=ALU.not_equal, fill=1.0, base=0,
                                        pattern=[[-1, P]], channel_multiplier=1).then_inc(s_const, 1)

            fc_res = psum[:, 0:D]
            res_fc = psum[:, 512:512 + D]
            aT = psum[0:D, 1024:1024 + 2 * H]
            ups = psum[:, 1536:1536 + 2 * H]

            @block.tensor
            def _(pe):
                pe.wait_ge(s_const, 6)
                pe.wait_ge(s_attn, 32)
                pe.wait_ge(s_w, 48)
                for m in range(2):
                    last = nc.tensor.transpose(aT[:, m * H:(m + 1) * H], attn_rows[:, m, :], ident[0:H, 0:H])
                last.then_inc(s_attn_t, 1)
                nc.tensor.transpose(fc_res, wtmp[:, 0:2, :].rearrange("e m d -> e (m d)"), ident[0:D, 0:D])
                nc.tensor.transpose(res_fc, wtmp[:, 1:3, :].rearrange("e m d -> e (m d)"), ident[0:D, 0:D]
                                    ).then_inc(s_wt, 1)
                pe.wait_ge(s_attn_c, 1)
                nc.tensor.matmul(ups[0:D, :], wtmp[0:D, 0, :], attn_cols[:, :, :].rearrange("p m h -> p (m h)"),
                                 start=True, stop=True)
                nc.tensor.matmul(ups[D:P, :], wtmp[0:D, 0, :], attn_cols[:, :, :].rearrange("p m h -> p (m h)"),
                                 start=True, stop=True).then_inc(s_u, 1)

            @block.vector
            def _(dve):
                dve.wait_ge(s_attn_t, 1)
                nc.vector.tensor_copy(attn_cols[:, :, :].rearrange("p m h -> p (m h)"), aT).then_inc(s_attn_c, 1)
                dve.wait_ge(s_wt, 1)
                dve.wait_ge(s_const, 6)
                nc.vector.tensor_copy(w_agg[0:D, 0:D], fc_res[0:D, :]).then_inc(s_wset, 1)
                nc.vector.tensor_copy(w_agg[D:P, D:P], res_fc[D:P, :]).then_inc(s_wset, 1)
                for c in range(C):
                    nc.vector.tensor_copy(w_node[0:D, c, 0:D], res_fc[0:D, :]).then_inc(s_wset, 1)
                    nc.vector.tensor_copy(w_node[D:P, c, D:2 * D], fc_res[D:P, :]).then_inc(s_wset, 1)
                dve.wait_ge(s_u, 1)
                for c in range(C):
                    for m in range(2):
                        for i in range(2):
                            nc.vector.tensor_copy(w_node[i * D:(i + 1) * D, c, 2 * D + 2 * (1 - m) + i:2 * D + 2 * (1 - m) + i + 1],
                                                  ups[i * D:(i + 1) * D, m * H + 2 * c + i:m * H + 2 * c + i + 1]
                                                  ).then_inc(s_uc, 1)

        with ExitStack() as phase:
            def buf(name, shape, dt=fp32):
                return phase.enter_context(nc.sbuf_tensor(name, shape, dt))

            xin = buf("xin", [P, S, 2, F])
            res = buf("res", [P, S, 2, F])
            terms = buf("terms", [P, S, 2, 4 * C])
            xT = buf("xT", [P, 2, F])
            junk = buf("junk", [P, 2, F])
            part = buf("part", [P, S, 2, 2])
            negmean = buf("negmean", [P, S, 2, 1])
            ssq = buf("ssq", [P, S, 2, 1])
            var = buf("var", [P, S, 2, 1])
            rstd = buf("rstd", [P, S, 2, 1])
            loaded = [sem(f"loaded{s}") for s in range(S)]
            stored = [sem(f"stored{s}") for s in range(S)]
            xT_ready, xT_copied, proj_ready, proj_used, terms_used = (sem(n) for n in
                ("xT_ready", "xT_copied", "proj_ready", "proj_used", "terms_used"))
            mean_ready, ssq_ready, var_ready, rstd_ready, out_ready = (sem(n) for n in
                ("mean_ready", "ssq_ready", "var_ready", "rstd_ready", "out_ready"))

            def xT_ps(t):
                return psum[:, (t % 2) * 1024:(t % 2) * 1024 + F]

            def proj_ps(t):
                at = 2048 + (t % 2) * 1024
                return psum[:, at:at + 1024].rearrange("p (b w) -> p b w", b=2)[:, :, 0:3 * PAIR].rearrange(
                    "p b (c w) -> p b c w", w=PAIR)

            def laps(eng, step, flush=None):
                full = (NG - 1) // S
                for s in range(S):
                    step(0, s)
                with eng.Fori(1, full) as lap:
                    for s in range(S):
                        step(lap, s)
                for s in range(NG - full * S):
                    step(full, s)
                if flush:
                    flush()

            def first_row(lap, s):
                return LAST0 if isinstance(lap, int) and S * lap + s == NG - 1 else lap * (S * G) + s * G

            def dram_rows(t, lap, s, n):
                return t[bass.ds(first_row(lap, s), G), :].rearrange("(p j) f -> p j f", j=2) if not isinstance(
                    lap, int) else t[first_row(lap, s):first_row(lap, s) + G, :].rearrange("(p j) f -> p j f", j=2)

            with nc.Block() as block:
                @block.sync
                def _(sp):
                    def step(lap, s):
                        wait(sp, proj_used, 2 * S * (lap - 1) + 2 * (s + 1))
                        sp.dma_start(xin[:, s], dram_rows(x, lap, s, F)).then_inc(loaded[s], 16)
                    laps(sp, step)

                @block.tensor
                def _(pe):
                    def project(lap, s, j):
                        t = 2 * s + j
                        wait(pe, xT_copied, 2 * S * lap + t + 1)
                        wait(pe, proj_used, 2 * S * lap + t - 1)
                        wait(pe, terms_used, 2 * S * lap + t - 1)
                        ps = proj_ps(t)
                        for c in range(C):
                            last = nc.tensor.matmul(ps[:, c // 3, c % 3, :], xT[:, t % 2, c * P:(c + 1) * P],
                                                    w_node[:, c, :], start=True, stop=True)
                        last.then_inc(proj_ready, 1)

                    def step(lap, s):
                        for j in range(2):
                            t = 2 * s + j
                            if j == 0:
                                pe.wait_ge(loaded[s], 16 * lap + 16)
                            wait(pe, xT_copied, 2 * S * lap + t - 1)
                            for c in range(C):
                                last = nc.tensor.transpose(xT_ps(t)[:, c * P:(c + 1) * P],
                                                           xin[:, s, j, c * P:(c + 1) * P], ident[:])
                            last.then_inc(xT_ready, 1)
                            if j:
                                project(lap, s, 0)
                            elif s:
                                project(lap, s - 1, 1)
                            elif not isinstance(lap, int) or lap:
                                project(lap - 1, S - 1, 1)
                    laps(pe, step, lambda: project((NG - 1) // S, (NG - 1) % S, 1))

                @block.scalar
                def _(act):
                    def square(lap, s, j):
                        t = 2 * s + j
                        act.wait_ge(mean_ready, 2 * S * lap + t + 1)
                        wait(act, ssq_ready, 2 * S * lap + t - 1)
                        nc.scalar.activation(junk[:, j, :], res[:, s, j, :], ACT.Square, bias=negmean[:, s, j, :],
                                             accum_out=ssq[:, s, j, :]).then_inc(ssq_ready, 1)

                    def step(lap, s):
                        for j in range(2):
                            t = 2 * s + j
                            act.wait_ge(xT_ready, 2 * S * lap + t + 1)
                            wait(act, proj_ready, 2 * S * lap + t - 1)
                            nc.scalar.copy(xT[:, t % 2, :], xT_ps(t)).then_inc(xT_copied, 1)
                            if j == 0 and (s or not isinstance(lap, int) or lap):
                                before = (lap, s - 1) if s else (lap - 1, S - 1)
                                square(*before, 0)
                                square(*before, 1)
                    def flush():
                        lap, s = (NG - 1) // S, (NG - 1) % S
                        square(lap, s, 0)
                        square(lap, s, 1)
                    laps(act, step, flush)

                @block.vector
                def _(dve):
                    def step(lap, s):
                        for j in range(2):
                            t = 2 * s + j
                            dve.wait_ge(proj_ready, 2 * S * lap + t + 1)
                            if j == 0:
                                wait(dve, stored[s], 32 * lap)
                            ps = proj_ps(t)
                            nc.vector.tensor_copy(terms[:, s, j, :].rearrange("p (b c w) -> p b c w", b=2, c=3),
                                                  ps[:, :, :, 2 * D:PAIR]).then_inc(terms_used, 1)
                            for b in range(2):
                                cut = slice(b * (F // 2), (b + 1) * (F // 2))
                                last = nc.vector.scalar_tensor_tensor(
                                    out=res[:, s, j, cut].rearrange("p (c w) -> p c w", c=3),
                                    in0=ps[:, b, :, 0:2 * D], scalar=0.0,
                                    in1=xin[:, s, j, cut].rearrange("p (c w) -> p c w", c=3),
                                    op0=ALU.max, op1=ALU.add, accum_out=part[:, s, j, b:b + 1])
                            last.then_inc(proj_used, 1)
                        if s or not isinstance(lap, int) or lap:
                            normalise(*((lap, s - 1) if s else (lap - 1, S - 1)))

                    def normalise(lap, s):
                        dve.wait_ge(rstd_ready, 2 * S * lap + 2 * s + 2)
                        for j in range(2):
                            nc.vector.tensor_scalar(res[:, s, j, :], res[:, s, j, :], negmean[:, s, j, :],
                                                    rstd[:, s, j, :], ALU.add, ALU.mult).then_inc(out_ready, 1)
                    laps(dve, step, lambda: normalise((NG - 1) // S, (NG - 1) % S))

                @block.gpsimd
                def _(pool):
                    def finish(lap, s):
                        hold(pool, ssq_ready, 2 * S * lap + 2 * s + 2)
                        nc.gpsimd.tensor_scalar(var[:, s], ssq[:, s], 1.0 / F, EPS, ALU.mult, ALU.add
                                                ).then_inc(var_ready, 1)
                        hold(pool, var_ready, S * lap + s + 1)
                        nc.gpsimd.tensor_tensor(rstd[:, s, :, 0], var[:, s, :, 0], half[:].to_broadcast([P, 2]),
                                                ALU.pow).then_inc(rstd_ready, 2)

                    def store(lap, s):
                        is_last = isinstance(lap, int) and S * lap + s == NG - 1
                        p0 = FRESH // 2 if is_last else 0
                        hold(pool, out_ready, 2 * S * lap + 2 * s + 2)
                        pool.dma_start(dram_rows(out, lap, s, F)[p0:P], res[p0:P, s]).then_inc(stored[s], 16)
                        pool.dma_start(dram_rows(table, lap, s, 4 * C)[p0:P], terms[p0:P, s]).then_inc(stored[s], 16)

                    def step(lap, s):
                        for j in range(2):
                            t = 2 * s + j
                            hold(pool, proj_used, 2 * S * lap + t + 1)
                            nc.gpsimd.tensor_scalar(negmean[:, s, j, :], part[:, s, j, 0:1], part[:, s, j, 1:2],
                                                    -1.0 / F, ALU.add, ALU.mult).then_inc(mean_ready, 1)
                        if s or not isinstance(lap, int) or lap:
                            finish(*((lap, s - 1) if s else (lap - 1, S - 1)))
                            if s > 1 or not isinstance(lap, int) or lap:
                                store(*((lap, s - 2) if s > 1 else (lap - 1, S + s - 2)))
                    def flush():
                        lap, s = (NG - 1) // S, (NG - 1) % S
                        finish(lap, s)
                        store(*((lap, s - 1) if s else (lap - 1, S - 1)))
                        store(lap, s)
                        for i in range(S):
                            pool.wait_ge(stored[i], 32 * (-(-(NG - i) // S)))
                    laps(pool, step, flush)

        with ExitStack() as phase:
            def buf(name, shape, dt=fp32):
                return phase.enter_context(nc.sbuf_tensor(name, shape, dt))

            E1 = F + H
            all_cols = buf("all_cols", [P, NBLK, 4], i32)
            same_next = buf("same_next", [P, NBLK])
            idx = buf("idx", [P, S, 4], i32)
            out_idx = buf("out_idx", [P, S], i32)
            dst_row = buf("dst_row", [P, S, P + 1], i32)
            xs = buf("xs", [P, S, E1])
            xd = buf("xd", [P, S, F])
            src_terms = buf("src_terms", [P, S, 4 * C])
            same = buf("same", [P, 2, P])
            far = buf("far", [H, 2, P + 1])
            apart = buf("apart", [H, 2, P + 2])
            xdT = buf("xdT", [P, 2, F])
            raw = buf("raw", [P, 2, H])
            score = buf("score", [P, 2, H])
            scoreT = buf("scoreT", [H, 2, P])
            ahead = buf("ahead", [H, 2, P])
            top = buf("top", [H, 2, P])
            below = buf("below", [H, 2, P])
            weightT = buf("weightT", [H, 2, P])
            weight = buf("weight", [P, 2, H])
            y = buf("y", [P, 2, E1])
            rden = buf("rden", [P, 2, H])
            zn = buf("zn", [P, 2, F])
            znT = buf("znT", [P, 2, F])
            res2 = buf("res2", [P, S, F])
            junk2 = buf("junk2", [P, 2, F])
            part2 = buf("part2", [P, S, 2])
            negmean2 = buf("negmean2", [P, S, 1])
            ssq2 = buf("ssq2", [P, S, 1])
            var2 = buf("var2", [P, S, 1])
            rstd2 = buf("rstd2", [P, S, 1])

            def proj(b):
                at = (b % 2) * 1024
                return psum[:, at:at + 1024].rearrange("p (b w) -> p b w", b=2)[:, :, 0:3 * (2 * D + 2)].rearrange(
                    "p b (c w) -> p b c w", w=2 * D + 2)

            turned = psum[:, 2048:2048 + F]
            z = psum[:, 3072:3072 + E1]
            scoreT_ps = psum[0:H, 2048 + F:2048 + F + P]
            weight_ps = psum[:, 2048 + F + P:2048 + F + P + H]

            (cols_in, sidx_a, sidx_set, cleared, ones_set) = (sem(n) for n in
                ("cols_in", "sidx_a", "sidx_set", "cleared", "ones_set"))
            rows_in, xs_in, xd_in, terms_in, out_done = ([sem(f"{n}{s}") for s in range(S)] for n in
                ("rows_in", "xs_in", "xd_in", "terms_in", "out_done"))
            (idx_set, same_set, far_set, apart_set, raw_set, score_set, max_carried, ahead_set, top_set, below_set,
             y_set, den_set, zn_set, res_set, norm_set) = (sem(n) for n in
                ("idx_set", "same_set", "far_set", "apart_set", "raw_set", "score_set", "max_carried", "ahead_set",
                 "top_set", "below_set", "y_set", "den_set", "zn_set", "res_set", "norm_set"))
            (xd_turned, resid_done, scoreT_done, weight_done, z_done, zn_turned, proj_done) = (sem(n) for n in
                ("xd_turned", "resid_done", "scoreT_done", "weight_done", "z_done", "zn_turned", "proj_done"))
            (weight_copied, xdT_copied, scoreT_copied, exp_done, sum_carried, znT_copied, ssq_set) = (sem(n) for n in
                ("weight_copied", "xdT_copied", "scoreT_copied", "exp_done", "sum_carried", "znT_copied", "ssq_set"))
            (out_idx_set, mean_set, var_set, rstd_set) = (sem(n) for n in ("out_idx_set", "mean_set", "var_set", "rstd_set"))

            class Blk:
                def __init__(self, lap, s):
                    self.lap, self.s = (lap, s) if 0 <= s < S else (lap + s // S, s % S)
                    self.n = self.s + S * self.lap
                    self.there = not isinstance(lap, int) or 0 <= self.n < NBLK
                    self.i = self.s % 2

                def uses(self, k=1):
                    return 16 * k * (self.lap + 1)

            def walk(eng, step, ahead_by=0, behind_by=0):
                def at(lap, s):
                    def blk(k=0):
                        b = Blk(lap, s + k)
                        return b if b.there else None
                    return blk
                full = (NBLK - 3) // S
                for s in range(-ahead_by, S):
                    step(at(0, s))
                with eng.Fori(1, full) as lap:
                    for s in range(S):
                        step(at(lap, s))
                for n in range(S * full, NBLK + behind_by):
                    step(at(full, n - S * full))

            with nc.Block() as block:
                @block.sync
                def _(sp):
                    sp.dma_start(all_cols[:], cols).then_inc(cols_in, 16)

                    def step(blk):
                        if b := blk():
                            hold(sp, apart_set, b.n - S + 1)
                            hold(sp, same_set, 2 * (b.n - S + 1))
                            row = rows[bass.ds(b.n, 1), :] if not isinstance(b.n, int) else rows[b.n:b.n + 1, :]
                            sp.dma_start(dst_row[:, b.s, :], row.to_broadcast([P, P + 1])).then_inc(rows_in[b.s], 16)
                    walk(sp, step)

                @block.gpsimd
                def _(pool):
                    nc.gpsimd.memset(xs[:, :, 0:F], 0.0).then_inc(cleared, 1)
                    nc.gpsimd.memset(xs[:, :, F:E1], 1.0).then_inc(cleared, 1)
                    nc.gpsimd.memset(xd[:], 0.0).then_inc(cleared, 1)
                    nc.gpsimd.memset(src_terms[:], 0.0).then_inc(cleared, 1)
                    nc.gpsimd.memset(apart[:], 0.0).then_inc(cleared, 1)
                    pool.wait_ge(cleared, 5)
                    nc.gpsimd.memset(xs[0:1, 0, F:E1], 0.0).then_inc(ones_set, 1)
                    pool.wait_ge(sidx_set, 1)
                    pool.wait_ge(ones_set, 1)

                    def load(b):
                        for used in (xd_in, terms_in, xs_in):
                            hold(pool, used[b.s], b.uses() - 16)
                        hold(pool, same_set, 2 * (b.n - S + 1))
                        col = all_cols[:, bass.ds(b.n, 1), :] if not isinstance(b.n, int) else all_cols[:, b.n:b.n + 1, :]
                        nc.gpsimd.tensor_copy(idx[:, b.s:b.s + 1, :], col).then_inc(idx_set, 1)
                        hold(pool, idx_set, b.n + 1)
                        for dest, table_, k, freed, count, done in (
                                (xd[:, b.s, :], x, 1, res_set, b.n - S + 1, xd_in),
                                (src_terms[:, b.s, :], table, 0, raw_set, b.n - S + 1, terms_in),
                                (xs[:, b.s, 0:F], x, 0, y_set, 2 * (b.n - S + 1), xs_in)):
                            if not (isinstance(count, int) and count <= 0):
                                hold(pool, freed, count)
                            nc.gpsimd.indirect_dma_start(
                                out=dest, out_offset=None, in_=table_,
                                in_offset=bass.IndirectOffsetOnAxis(ap=idx[:, b.s, k:k + 1], axis=0),
                                bounds_check=N - 1, oob_is_err=False).then_inc(done[b.s], 16)

                    def step(blk):
                        if b := blk(2):
                            load(b)
                        if b := blk(-1):
                            hold(pool, res_set, b.n + 1)
                            nc.gpsimd.tensor_scalar(negmean2[:, b.s, :], part2[:, b.s, 0:1], part2[:, b.s, 1:2],
                                                    -1.0 / F, ALU.add, ALU.mult).then_inc(mean_set, 1)
                            hold(pool, ssq_set, b.n + 1)
                            nc.gpsimd.tensor_scalar(var2[:, b.s, :], ssq2[:, b.s, :], 1.0 / F, EPS, ALU.mult, ALU.add
                                                    ).then_inc(var_set, 1)
                            hold(pool, var_set, b.n + 1)
                            nc.gpsimd.tensor_tensor(rstd2[:, b.s, :], var2[:, b.s, :], half[:], ALU.pow
                                                    ).then_inc(rstd_set, 1)
                        if b := blk(-2):
                            hold(pool, out_done[b.s], b.uses() - 16)
                            col = (all_cols[:, bass.ds(b.n, 1), 3] if not isinstance(b.n, int) else
                                   all_cols[:, b.n:b.n + 1, 3])
                            nc.gpsimd.tensor_copy(out_idx[:, b.s:b.s + 1], col).then_inc(out_idx_set, 1)
                            hold(pool, out_idx_set, b.n + 1)
                            hold(pool, norm_set, b.n + 1)
                            nc.gpsimd.indirect_dma_start(
                                out=out, out_offset=bass.IndirectOffsetOnAxis(ap=out_idx[:, b.s:b.s + 1], axis=0),
                                in_=res2[:, b.s, :], in_offset=None,
                                bounds_check=N - 1, oob_is_err=False).then_inc(out_done[b.s], 16)
                    walk(pool, step, 2, 2)
                    for s in range(S):
                        pool.wait_ge(out_done[s], 16 * (-(-(NBLK - s) // S)))

                @block.tensor
                def _(pe):
                    def step(blk):
                        if b := blk(1):
                            pe.wait_ge(xd_in[b.s], b.uses())
                            wait(pe, znT_copied, b.n - 1)
                            wait(pe, weight_copied, b.n)
                            for c in range(C):
                                last = nc.tensor.transpose(turned[:, c * P:(c + 1) * P],
                                                           xd[:, b.s, c * P:(c + 1) * P], ident[:])
                            last.then_inc(xd_turned, 1)
                        if b := blk():
                            pe.wait_ge(y_set, 2 * (b.n + 1))
                            pe.wait_ge(same_set, 2 * (b.n + 1))
                            wait(pe, zn_set, b.n)
                            wait(pe, sum_carried, b.n)
                            nc.tensor.matmul(z[:, 0:512], same[:, b.i, :], y[:, b.i, 0:512], start=True, stop=True)
                            nc.tensor.matmul(z[:, 512:E1], same[:, b.i, :], y[:, b.i, 512:E1], start=True, stop=True
                                             ).then_inc(z_done, 1)
                        if b := blk(1):
                            pe.wait_ge(xdT_copied, b.n + 1)
                            wait(pe, res_set, b.n - 1)
                            ps = proj(b.i)
                            for c in range(C):
                                last = nc.tensor.matmul(ps[:, c // 3, c % 3, :], xdT[:, b.i, c * P:(c + 1) * P],
                                                        w_node[:, c, 0:2 * D + 2], start=(c % 3 == 0), stop=(c % 3 == 2))
                            last.then_inc(resid_done, 1)
                        if b := blk():
                            pe.wait_ge(zn_set, b.n + 1)
                            if blk(1):
                                pe.wait_ge(xdT_copied, b.n + 2)
                            for c in range(C):
                                last = nc.tensor.transpose(turned[:, c * P:(c + 1) * P],
                                                           zn[:, b.i, c * P:(c + 1) * P], ident[:])
                            last.then_inc(zn_turned, 1)
                        if b := blk(1):
                            pe.wait_ge(score_set, b.n + 1)
                            if blk():
                                pe.wait_ge(znT_copied, b.n)
                            nc.tensor.transpose(scoreT_ps, score[:, b.i, :], ident[:]).then_inc(scoreT_done, 1)
                        if b := blk():
                            pe.wait_ge(znT_copied, b.n + 1)
                            ps = proj(b.i)
                            for c in range(C):
                                last = nc.tensor.matmul(ps[:, c // 3, c % 3, 0:2 * D], znT[:, b.i, c * P:(c + 1) * P],
                                                        w_agg[:], start=False, stop=(c % 3 == 2),
                                                        skip_group_check=True)
                            last.then_inc(proj_done, 1)
                        if b := blk(1):
                            hold(pe, exp_done, b.n + 1)
                            nc.tensor.transpose(weight_ps, weightT[:, b.i, :], ident[0:H, 0:H]).then_inc(weight_done, 1)
                    walk(pe, step, 1)

                @block.scalar
                def _(act):
                    def step(blk):
                        if b := blk(1):
                            act.wait_ge(xd_turned, b.n + 1)
                            wait(act, resid_done, b.n - 1)
                            nc.scalar.copy(xdT[:, b.i, :], turned).then_inc(xdT_copied, 1)
                        if b := blk():
                            act.wait_ge(z_done, b.n + 1)
                            if nxt := blk(1):
                                act.wait_ge(xs_in[nxt.s], nxt.uses())
                                nc.scalar.copy(xs[0:1, nxt.s, :], z[0:1, :]).then_inc(sum_carried, 1)
                            act.wait_ge(zn_turned, b.n + 1)
                            wait(act, proj_done, b.n - 1)
                            nc.scalar.copy(znT[:, b.i, :], turned).then_inc(znT_copied, 1)
                        if b := blk(1):
                            act.wait_ge(scoreT_done, b.n + 1)
                            wait(act, below_set, b.n - 1)
                            nc.scalar.copy(scoreT[:, b.i, 1:P], scoreT_ps[:, 1:P]).then_inc(scoreT_copied, 1)
                            act.wait_ge(below_set, b.n + 1)
                            wait(act, weight_done, b.n - 1)
                            nc.scalar.activation(weightT[:, b.i, :], below[:, b.i, :], ACT.Exp).then_inc(exp_done, 1)
                            act.wait_ge(weight_done, b.n + 1)
                            wait(act, y_set, 2 * (b.n - 1))
                            nc.scalar.copy(weight[:, b.i, :], weight_ps).then_inc(weight_copied, 1)
                        if b := blk(-1):
                            act.wait_ge(mean_set, b.n + 1)
                            wait(act, ssq_set, b.n - 1)
                            nc.scalar.activation(junk2[:, b.i, :], res2[:, b.s, :], ACT.Square,
                                                 bias=negmean2[:, b.s, :], accum_out=ssq2[:, b.s, :]
                                                 ).then_inc(ssq_set, 1)
                    walk(act, step, 1, 1)

                @block.vector
                def _(dve):
                    dve.wait_ge(cols_in, 16)
                    nc.vector.tensor_tensor(same_next[:], all_cols[:, :, 2], all_cols[:, :, 3], ALU.is_equal
                                            ).then_inc(sidx_a, 1)
                    dve.wait_ge(sidx_a, 1)
                    nc.vector.scalar_tensor_tensor(out=all_cols[:, :, 3], in0=same_next[:], scalar=float(BIG),
                                                   in1=all_cols[:, :, 1], op0=ALU.mult, op1=ALU.add
                                                   ).then_inc(sidx_set, 1)
                    dve.wait_ge(cleared, 5)
                    dve.wait_ge(ones_set, 1)
                    nc.vector.memset(top[:, 1, P - 1:P], 0.0).then_inc(ones_set, 1)
                    dve.wait_ge(ones_set, 2)

                    def step(blk):
                        if b := blk():
                            dve.wait_ge(weight_copied, b.n + 1)
                            dve.wait_ge(xs_in[b.s], b.uses())
                            wait(dve, sum_carried, b.n)
                            wait(dve, z_done, b.n - 1)
                            nc.vector.tensor_tensor(
                                y[:, b.i, 0:F].rearrange("p (h d) -> p h d", d=D),
                                xs[:, b.s, 0:F].rearrange("p (h d) -> p h d", d=D),
                                weight[:, b.i, :].unsqueeze(2).to_broadcast([P, H, D]), ALU.mult).then_inc(y_set, 1)
                            nc.vector.tensor_tensor(y[:, b.i, F:E1], xs[:, b.s, F:E1], weight[:, b.i, :], ALU.mult
                                                    ).then_inc(y_set, 1)
                        if b := blk(-1):
                            dve.wait_ge(proj_done, b.n + 1)
                            wait(dve, out_done[b.s], b.uses() - 16)
                            ps = proj(b.i)
                            for k in range(2):
                                cut = slice(k * (F // 2), (k + 1) * (F // 2))
                                last = nc.vector.scalar_tensor_tensor(
                                    out=res2[:, b.s, cut].rearrange("p (c w) -> p c w", c=3),
                                    in0=ps[:, k, :, 0:2 * D], scalar=0.0,
                                    in1=xd[:, b.s, cut].rearrange("p (c w) -> p c w", c=3),
                                    op0=ALU.max, op1=ALU.add, accum_out=part2[:, b.s, k:k + 1])
                            last.then_inc(res_set, 1)
                        if b := blk(1):
                            dve.wait_ge(rows_in[b.s], b.uses())
                            dve.wait_ge(idx_set, b.n + 1)
                            wait(dve, z_done, b.n - 1)
                            nc.vector.tensor_scalar(same[:, b.i, 1:P], dst_row[:, b.s, 1:P], idx[:, b.s, 2:3], None,
                                                    ALU.is_equal).then_inc(same_set, 1)
                            nc.vector.tensor_scalar(same[:, b.i, 0:1], dst_row[:, b.s, P - 1:P], idx[:, b.s, 2:3],
                                                    None, ALU.is_equal).then_inc(same_set, 1)
                            wait(dve, apart_set, b.n - 1)
                            nc.vector.tensor_scalar(far[:, b.i, :], dst_row[0:H, b.s, :], APART, None, ALU.mult
                                                    ).then_inc(far_set, 1)
                            dve.wait_ge(far_set, b.n + 1)
                            wait(dve, top_set, b.n - 1)
                            nc.vector.tensor_tensor(apart[:, b.i, 1:P + 1], far[:, b.i, 0:P], far[:, b.i, 1:P + 1],
                                                    ALU.subtract).then_inc(apart_set, 1)
                        if b := blk():
                            dve.wait_ge(z_done, b.n + 1)
                            if blk(1):
                                dve.wait_ge(sum_carried, b.n + 1)
                            wait(dve, zn_set, b.n - 1)
                            nc.vector.reciprocal(rden[:, b.i, :], z[:, F:E1]).then_inc(den_set, 1)
                            dve.wait_ge(den_set, b.n + 1)
                            wait(dve, zn_turned, b.n - 1)
                            nc.vector.tensor_tensor(
                                zn[:, b.i, :].rearrange("p (h d) -> p h d", d=D),
                                z[:, 0:F].rearrange("p (h d) -> p h d", d=D),
                                rden[:, b.i, :].unsqueeze(2).to_broadcast([P, H, D]), ALU.mult).then_inc(zn_set, 1)
                        if b := blk(1):
                            dve.wait_ge(resid_done, b.n + 1)
                            dve.wait_ge(terms_in[b.s], b.uses())
                            wait(dve, score_set, b.n - 1)
                            nc.vector.tensor_tensor(
                                raw[:, b.i, :].rearrange("p (a c m) -> p a c m", a=2, m=2),
                                proj(b.i)[:, :, :, 2 * D:2 * D + 2],
                                src_terms[:, b.s, :].rearrange("p (a c w) -> p a c w", a=2, w=4)[:, :, :, 2:4],
                                ALU.add).then_inc(raw_set, 1)
                            dve.wait_ge(raw_set, b.n + 1)
                            wait(dve, scoreT_done, b.n - 1)
                            nc.vector.scalar_tensor_tensor(out=score[:, b.i, :], in0=raw[:, b.i, :], scalar=SLOPE,
                                                           in1=raw[:, b.i, :], op0=ALU.mult, op1=ALU.max
                                                           ).then_inc(score_set, 1)
                            wait(dve, below_set, b.n - 1)
                            wait(dve, top_set, b.n)
                            nc.vector.tensor_copy(scoreT[:, b.i, 0:1], top[:, 1 - b.i, P - 1:P]
                                                  ).then_inc(max_carried, 1)
                            dve.wait_ge(max_carried, b.n + 1)
                            dve.wait_ge(scoreT_copied, b.n + 1)
                            dve.wait_ge(apart_set, b.n + 1)
                            nc.vector.tensor_tensor_scan(ahead[:, b.i, :], apart[:, b.i, 0:P], scoreT[:, b.i, :],
                                                         LOWEST, ALU.add, ALU.max).then_inc(ahead_set, 1)
                            dve.wait_ge(ahead_set, b.n + 1)
                            wait(dve, exp_done, b.n - 1)
                            nc.vector.tensor_tensor_scan(top[:, b.i, ::-1], apart[:, b.i, P:0:-1],
                                                         ahead[:, b.i, ::-1], LOWEST, ALU.add, ALU.max
                                                         ).then_inc(top_set, 1)
                            dve.wait_ge(top_set, b.n + 1)
                            nc.vector.tensor_tensor(below[:, b.i, :], scoreT[:, b.i, :], top[:, b.i, :], ALU.subtract
                                                    ).then_inc(below_set, 1)
                        if b := blk(-1):
                            dve.wait_ge(rstd_set, b.n + 1)
                            nc.vector.tensor_scalar(res2[:, b.s, :], res2[:, b.s, :], negmean2[:, b.s, :],
                                                    rstd2[:, b.s, :], ALU.add, ALU.mult).then_inc(norm_set, 1)
                    walk(dve, step, 1, 1)

_INS = ['x', 'L0_gnn_W_fc', 'L0_gnn_attn_l', 'L0_gnn_attn_r', 'L0_gnn_W_res']


def kernel(**inputs):
    import numpy as _np
    import concourse.bacc as _bacc
    from concourse import mybir as _mybir
    from concourse.bass_utils import run_bass_kernel_spmd as _run

    x = _np.ascontiguousarray(inputs['x'])
    src, dst = _np.asarray(inputs['src']), _np.asarray(inputs['dst'])
    n, e = x.shape[0], src.shape[0]
    blocks = -(-e // EB)
    pad = blocks * EB - e
    none = _np.full((1,), n, src.dtype)
    srcs = _np.concatenate([none, src, _np.full((pad + 1,), n, src.dtype)])
    dsts = _np.concatenate([_np.full((1,), -1, dst.dtype), dst, _np.full((pad + 1,), n, dst.dtype)])
    at = EB * _np.arange(blocks)[None, :] + _np.arange(P)[:, None]
    cols = _np.stack([srcs[at], dsts[at], dsts[at], dsts[at + 1]], axis=-1)
    cols[0, :, 0:2] = n
    cols[0, :, 3] = cols[0, :, 2]
    rows = dsts[EB * _np.arange(blocks)[:, None] + _np.arange(P + 1)[None, :]]

    nc = _bacc.Bacc("TRN2", target_bir_lowering=False, num_devices=1)
    named = {k: _np.ascontiguousarray(inputs[k]) for k in _INS}
    named['edge_cols'], named['dst_rows'] = _np.ascontiguousarray(cols), _np.ascontiguousarray(rows)
    arrays, args = {}, []
    for name, a in named.items():
        arrays[f"in_{name}_dram"] = a
        args.append(nc.dram_tensor(f"in_{name}_dram", a.shape, _mybir.dt.from_np(a.dtype), kind="ExternalInput").ap())
    args.append(nc.dram_tensor("out_0_dram", x.shape, _mybir.dt.float32, kind="ExternalOutput").ap())
    gnn_program(nc, *args)
    r = _run(nc, [arrays], core_ids=[0])
    return r.results[0]["out_0_dram"]
```

```python
from contextlib import ExitStack

import concourse.bass as bass
from concourse import mybir

H, D = 12, 64
F = H * D
P = 128
C = F // P
PAIR = 2 * D + 4
EPS = 1e-5
SLOPE = 0.2
BIG = 1 << 20
APART = 1.0e33
LOWEST = -2.0e38


def gnn_program(nc, x, W_fc, attn_l, attn_r, W_res, cols, rows, out, LEVELS):
    fp32, i32 = mybir.dt.float32, mybir.dt.int32
    ALU, ACT = mybir.AluOpType, mybir.ActivationFunctionType
    N = x.shape[0]
    G = 2 * P
    NG = -(-N // G)
    LAST0 = N - G
    FRESH = (NG - 1) * G - LAST0
    S = 6
    LAG = 6
    NBLK = sum(LEVELS)
    RP = next(p for p in range(P, 0, -1) if NBLK % p == 0)

    apart_rows = nc.dram_tensor("apart_rows", [NBLK, P], fp32).ap()
    table = nc.dram_tensor("attention_terms", [N, 4 * C], fp32).ap()

    ctx = ExitStack()
    with ctx:
        def sb(name, shape, dt=fp32):
            return ctx.enter_context(nc.sbuf_tensor(name, shape, dt))

        def sem(name):
            return ctx.enter_context(nc.semaphore(name))

        def wait(eng, s, value):
            if not (isinstance(value, int) and value <= 0):
                eng.wait_ge(s, value)

        def hold(eng, s, value):
            if not (isinstance(value, int) and value <= 0):
                eng.wait_ge(s, value)
                eng.sem_inc(held, 1)

        psum = ctx.enter_context(nc.psum_tensor("psum", [P, 8 * 512], fp32))
        ident = sb("ident", [P, P])
        wtmp = sb("wtmp", [D, 3, D])
        attn_rows = sb("attn_rows", [H, 2, D])
        attn_cols = sb("attn_cols", [D, 2, H])
        w_node = sb("w_node", [P, C, PAIR])
        w_agg = sb("w_agg", [P, P])
        half = sb("half", [P, 1])
        all_cols = sb("all_cols", [P, NBLK, 5], i32)

        held = sem("held")
        s_const, s_w, s_attn = sem("s_const"), sem("s_w"), sem("s_attn")
        s_attn_t, s_attn_c, s_wt, s_wset, s_u, s_uc = (sem(n) for n in
            ("s_attn_t", "s_attn_c", "s_wt", "s_wset", "s_u", "s_uc"))
        with nc.Block() as block:
            @block.sync
            def _(sp):
                for m, w in enumerate((W_fc, W_res, W_fc)):
                    sp.dma_start(wtmp[:, m, :], w).then_inc(s_w, 16)
                for m, a in enumerate((attn_l, attn_r)):
                    sp.dma_start(attn_rows[:, m, :], a).then_inc(s_attn, 16)

            @block.gpsimd
            def _(pool):
                nc.gpsimd.memset(ident[:], 0.0).then_inc(s_const, 1)
                nc.gpsimd.memset(half[:], -0.5).then_inc(s_const, 1)
                nc.gpsimd.memset(w_node[:], 0.0).then_inc(s_const, 1)
                nc.gpsimd.memset(w_agg[:], 0.0).then_inc(s_const, 1)
                pool.wait_ge(s_const, 4)
                nc.gpsimd.affine_select(out=ident[:], in_=ident[:], compare_op=ALU.not_equal, fill=1.0, base=0,
                                        pattern=[[-1, P]], channel_multiplier=1).then_inc(s_const, 1)

            fc_res = psum[:, 0:D]
            res_fc = psum[:, 512:512 + D]
            aT = psum[0:D, 1024:1024 + 2 * H]
            ups = psum[:, 1536:1536 + 2 * H]

            @block.tensor
            def _(pe):
                pe.wait_ge(s_const, 5)
                pe.wait_ge(s_attn, 32)
                pe.wait_ge(s_w, 48)
                for m in range(2):
                    last = nc.tensor.transpose(aT[:, m * H:(m + 1) * H], attn_rows[:, m, :], ident[0:H, 0:H])
                last.then_inc(s_attn_t, 1)
                nc.tensor.transpose(fc_res, wtmp[:, 0:2, :].rearrange("e m d -> e (m d)"), ident[0:D, 0:D])
                nc.tensor.transpose(res_fc, wtmp[:, 1:3, :].rearrange("e m d -> e (m d)"), ident[0:D, 0:D]
                                    ).then_inc(s_wt, 1)
                pe.wait_ge(s_attn_c, 1)
                nc.tensor.matmul(ups[0:D, :], wtmp[0:D, 0, :], attn_cols[:, :, :].rearrange("p m h -> p (m h)"),
                                 start=True, stop=True)
                nc.tensor.matmul(ups[D:P, :], wtmp[0:D, 0, :], attn_cols[:, :, :].rearrange("p m h -> p (m h)"),
                                 start=True, stop=True).then_inc(s_u, 1)

            @block.vector
            def _(dve):
                dve.wait_ge(s_attn_t, 1)
                nc.vector.tensor_copy(attn_cols[:, :, :].rearrange("p m h -> p (m h)"), aT).then_inc(s_attn_c, 1)
                dve.wait_ge(s_wt, 1)
                dve.wait_ge(s_const, 5)
                nc.vector.tensor_copy(w_agg[0:D, 0:D], fc_res[0:D, :]).then_inc(s_wset, 1)
                nc.vector.tensor_copy(w_agg[D:P, D:P], res_fc[D:P, :]).then_inc(s_wset, 1)
                for c in range(C):
                    nc.vector.tensor_copy(w_node[0:D, c, 0:D], res_fc[0:D, :]).then_inc(s_wset, 1)
                    nc.vector.tensor_copy(w_node[D:P, c, D:2 * D], fc_res[D:P, :]).then_inc(s_wset, 1)
                dve.wait_ge(s_u, 1)
                for c in range(C):
                    for m in range(2):
                        for i in range(2):
                            nc.vector.tensor_copy(w_node[i * D:(i + 1) * D, c, 2 * D + 2 * (1 - m) + i:2 * D + 2 * (1 - m) + i + 1],
                                                  ups[i * D:(i + 1) * D, m * H + 2 * c + i:m * H + 2 * c + i + 1]
                                                  ).then_inc(s_uc, 1)

        with ExitStack() as phase:
            def buf(name, shape, dt=fp32):
                return phase.enter_context(nc.sbuf_tensor(name, shape, dt))

            xin = buf("xin", [P, S, 2, F])
            res = buf("res", [P, S, 2, F])
            terms = buf("terms", [P, S, 2, 4 * C])
            xT = buf("xT", [P, 2, F])
            junk = buf("junk", [P, 2, F])
            part = buf("part", [P, S, 2, 2])
            negmean = buf("negmean", [P, S, 2, 1])
            ssq = buf("ssq", [P, S, 2, 1])
            var = buf("var", [P, S, 2, 1])
            rstd = buf("rstd", [P, S, 2, 1])
            loaded = [sem(f"loaded{s}") for s in range(S)]
            stored = [sem(f"stored{s}") for s in range(S)]
            xT_ready, xT_copied, proj_ready, proj_used, terms_used = (sem(n) for n in
                ("xT_ready", "xT_copied", "proj_ready", "proj_used", "terms_used"))
            mean_ready, ssq_ready, var_ready, rstd_ready, out_ready = (sem(n) for n in
                ("mean_ready", "ssq_ready", "var_ready", "rstd_ready", "out_ready"))

            flag = buf("flag", [P, 3, NBLK])
            rows_sb = buf("rows_sb", [RP, NBLK // RP, P + 1], i32)
            far = buf("far", [RP, NBLK // RP, P + 1])
            apart_sb = buf("apart_sb", [RP, NBLK // RP, P])
            cols_in, all_rows_in, flags_set, held_back_set, idx_ready, far_set, apart_done, apart_out = (sem(n) for n in
                ("cols_in", "all_rows_in", "flags_set", "held_back_set", "idx_ready", "far_set", "apart_done",
                 "apart_out"))

            def xT_ps(t):
                return psum[:, (t % 2) * 1024:(t % 2) * 1024 + F]

            def proj_ps(t):
                at = 2048 + (t % 2) * 1024
                return psum[:, at:at + 1024].rearrange("p (b w) -> p b w", b=2)[:, :, 0:3 * PAIR].rearrange(
                    "p b (c w) -> p b c w", w=PAIR)

            def laps(eng, step, flush=None):
                full = (NG - 1) // S
                for s in range(S):
                    step(0, s)
                with eng.Fori(1, full) as lap:
                    for s in range(S):
                        step(lap, s)
                for s in range(NG - full * S):
                    step(full, s)
                if flush:
                    flush()

            def first_row(lap, s):
                return LAST0 if isinstance(lap, int) and S * lap + s == NG - 1 else lap * (S * G) + s * G

            def dram_rows(t, lap, s, n):
                return t[bass.ds(first_row(lap, s), G), :].rearrange("(p j) f -> p j f", j=2) if not isinstance(
                    lap, int) else t[first_row(lap, s):first_row(lap, s) + G, :].rearrange("(p j) f -> p j f", j=2)

            with nc.Block() as block:
                @block.sync
                def _(sp):
                    def store(lap, s):
                        is_last = isinstance(lap, int) and S * lap + s == NG - 1
                        p0 = FRESH // 2 if is_last else 0
                        hold(sp, out_ready, 2 * S * lap + 2 * s + 2)
                        sp.dma_start(dram_rows(out, lap, s, F)[p0:P], res[p0:P, s]).then_inc(stored[s], 16)
                        sp.dma_start(dram_rows(table, lap, s, 4 * C)[p0:P], terms[p0:P, s]).then_inc(stored[s], 16)

                    def step(lap, s):
                        hold(sp, proj_used, 2 * S * (lap - 1) + 2 * (s + 1))
                        sp.dma_start(xin[:, s], dram_rows(x, lap, s, F)).then_inc(loaded[s], 16)
                        if isinstance(lap, int) and S * lap + s == S - 1:
                            sp.dma_start(all_cols[:], cols).then_inc(cols_in, 16)
                            sp.dma_start(rows_sb[:], rows.rearrange("(p k) w -> p k w", p=RP)).then_inc(all_rows_in, 16)
                        if not isinstance(lap, int) or S * lap + s >= LAG:
                            store(lap - (LAG - s + S - 1) // S, (s - LAG) % S)

                    def flush():
                        sp.wait_ge(apart_done, 1)
                        sp.dma_start(apart_rows.rearrange("(p k) w -> p k w", p=RP), apart_sb[:]).then_inc(apart_out, 16)
                        for g in range(NG - LAG, NG):
                            store(g // S, g % S)
                        sp.wait_ge(apart_out, 16)
                        for i in range(S):
                            sp.wait_ge(stored[i], 32 * (-(-(NG - i) // S)))
                    laps(sp, step, flush)

                @block.tensor
                def _(pe):
                    def project(lap, s, j):
                        t = 2 * s + j
                        wait(pe, xT_copied, 2 * S * lap + t + 1)
                        wait(pe, proj_used, 2 * S * lap + t - 1)
                        wait(pe, terms_used, 2 * S * lap + t - 1)
                        ps = proj_ps(t)
                        for c in range(C):
                            last = nc.tensor.matmul(ps[:, c // 3, c % 3, :], xT[:, t % 2, c * P:(c + 1) * P],
                                                    w_node[:, c, :], start=True, stop=True)
                        last.then_inc(proj_ready, 1)

                    def step(lap, s):
                        for j in range(2):
                            t = 2 * s + j
                            if j == 0:
                                pe.wait_ge(loaded[s], 16 * lap + 16)
                            wait(pe, xT_copied, 2 * S * lap + t - 1)
                            for c in range(C):
                                last = nc.tensor.transpose(xT_ps(t)[:, c * P:(c + 1) * P],
                                                           xin[:, s, j, c * P:(c + 1) * P], ident[:])
                            last.then_inc(xT_ready, 1)
                            if j:
                                project(lap, s, 0)
                            elif s:
                                project(lap, s - 1, 1)
                            elif not isinstance(lap, int) or lap:
                                project(lap - 1, S - 1, 1)
                    laps(pe, step, lambda: project((NG - 1) // S, (NG - 1) % S, 1))

                @block.scalar
                def _(act):
                    def square(lap, s, j):
                        t = 2 * s + j
                        act.wait_ge(mean_ready, 2 * S * lap + t + 1)
                        wait(act, ssq_ready, 2 * S * lap + t - 1)
                        nc.scalar.activation(junk[:, j, :], res[:, s, j, :], ACT.Square, bias=negmean[:, s, j, :],
                                             accum_out=ssq[:, s, j, :]).then_inc(ssq_ready, 1)

                    def step(lap, s):
                        for j in range(2):
                            t = 2 * s + j
                            act.wait_ge(xT_ready, 2 * S * lap + t + 1)
                            wait(act, proj_ready, 2 * S * lap + t - 1)
                            nc.scalar.copy(xT[:, t % 2, :], xT_ps(t)).then_inc(xT_copied, 1)
                            if s or not isinstance(lap, int) or lap:
                                square(*((lap, s - 1) if s else (lap - 1, S - 1)), j)
                    def flush():
                        lap, s = (NG - 1) // S, (NG - 1) % S
                        square(lap, s, 0)
                        square(lap, s, 1)
                    laps(act, step, flush)

                @block.vector
                def _(dve):
                    def step(lap, s):
                        for j in range(2):
                            t = 2 * s + j
                            dve.wait_ge(proj_ready, 2 * S * lap + t + 1)
                            if j == 0:
                                wait(dve, stored[s], 32 * lap)
                            ps = proj_ps(t)
                            nc.vector.tensor_copy(terms[:, s, j, :].rearrange("p (b c w) -> p b c w", b=2, c=3),
                                                  ps[:, :, :, 2 * D:PAIR]).then_inc(terms_used, 1)
                            for b in range(2):
                                cut = slice(b * (F // 2), (b + 1) * (F // 2))
                                last = nc.vector.scalar_tensor_tensor(
                                    out=res[:, s, j, cut].rearrange("p (c w) -> p c w", c=3),
                                    in0=ps[:, b, :, 0:2 * D], scalar=0.0,
                                    in1=xin[:, s, j, cut].rearrange("p (c w) -> p c w", c=3),
                                    op0=ALU.max, op1=ALU.add, accum_out=part[:, s, j, b:b + 1])
                            last.then_inc(proj_used, 1)
                            if s > 1 or not isinstance(lap, int) or lap:
                                normalise(*((lap, s - 2) if s > 1 else (lap - 1, s + S - 2)), j)
                        if isinstance(lap, int) and S * lap + s == S - 1:
                            prepare_edges()

                    def prepare_edges():
                        dve.wait_ge(cols_in, 16)
                        for k in range(3):
                            nc.vector.tensor_tensor(flag[:, k, :], all_cols[:, :, 1], all_cols[:, :, 2 + k], ALU.is_equal
                                                    ).then_inc(flags_set, 1)
                        dve.wait_ge(flags_set, 3)
                        nc.vector.tensor_scalar(all_cols[:, :, 3], flag[:, 1, :], 0.0, None, ALU.is_equal
                                                ).then_inc(held_back_set, 1)
                        nc.vector.tensor_tensor(flag[:, 0, :], flag[:, 0, :], flag[:, 1, :], ALU.add).then_inc(flags_set, 1)
                        dve.wait_ge(flags_set, 4)
                        dve.wait_ge(held_back_set, 1)
                        nc.vector.memset(all_cols[0:1, :, 3], 1).then_inc(idx_ready, 1)
                        nc.vector.tensor_tensor(flag[:, 0, :], flag[:, 0, :], flag[:, 2, :], ALU.add).then_inc(flags_set, 1)
                        dve.wait_ge(flags_set, 5)
                        nc.vector.scalar_tensor_tensor(out=all_cols[:, :, 2], in0=flag[:, 0, :], scalar=float(BIG),
                                                       in1=all_cols[:, :, 1], op0=ALU.mult, op1=ALU.add
                                                       ).then_inc(idx_ready, 1)
                        dve.wait_ge(all_rows_in, 16)
                        nc.vector.tensor_scalar(far[:], rows_sb[:], APART, None, ALU.mult).then_inc(far_set, 1)
                        dve.wait_ge(far_set, 1)
                        nc.vector.tensor_tensor(apart_sb[:], far[:, :, 0:P], far[:, :, 1:P + 1], ALU.subtract
                                                ).then_inc(apart_done, 1)

                    def normalise(lap, s, j):
                        dve.wait_ge(rstd_ready, 2 * S * lap + 2 * s + 2)
                        nc.vector.tensor_scalar(res[:, s, j, :], res[:, s, j, :], negmean[:, s, j, :],
                                                rstd[:, s, j, :], ALU.add, ALU.mult).then_inc(out_ready, 1)

                    def flush():
                        for g in (NG - 2, NG - 1):
                            normalise(g // S, g % S, 0)
                            normalise(g // S, g % S, 1)
                    laps(dve, step, flush)

                @block.gpsimd
                def _(pool):
                    def finish(lap, s):
                        hold(pool, ssq_ready, 2 * S * lap + 2 * s + 2)
                        nc.gpsimd.tensor_scalar(var[:, s], ssq[:, s], 1.0 / F, EPS, ALU.mult, ALU.add
                                                ).then_inc(var_ready, 1)
                        hold(pool, var_ready, S * lap + s + 1)
                        nc.gpsimd.tensor_tensor(rstd[:, s, :, 0], var[:, s, :, 0], half[:].to_broadcast([P, 2]),
                                                ALU.pow).then_inc(rstd_ready, 2)

                    def step(lap, s):
                        for j in range(2):
                            t = 2 * s + j
                            hold(pool, proj_used, 2 * S * lap + t + 1)
                            nc.gpsimd.tensor_scalar(negmean[:, s, j, :], part[:, s, j, 0:1], part[:, s, j, 1:2],
                                                    -1.0 / F, ALU.add, ALU.mult).then_inc(mean_ready, 1)
                        if s or not isinstance(lap, int) or lap:
                            finish(*((lap, s - 1) if s else (lap - 1, S - 1)))
                    def flush():
                        lap, s = (NG - 1) // S, (NG - 1) % S
                        finish(lap, s)
                    laps(pool, step, flush)

        FIRST = [sum(LEVELS[:k]) for k in range(len(LEVELS))]
        with ExitStack() as phase:
            def buf(name, shape, dt=fp32):
                return phase.enter_context(nc.sbuf_tensor(name, shape, dt))

            R = 8
            passed_terms = [nc.dram_tensor(f"passed_terms{k}", [2 * m, 2 * H], fp32).ap()
                            for k, m in enumerate(LEVELS[:-1])]
            passed_sums = [buf(f"passed_sums{k}", [P, C, 2 * m]) for k, m in enumerate(LEVELS[:-1])]

            idx = buf("idx", [P, R, 5], i32)
            out_idx = buf("out_idx", [P, R], i32)
            dst_row = buf("dst_row", [P, R, P], i32)
            apart = buf("apart", [H, R, P + 1])
            xs = buf("xs", [P, R, F])
            xd = buf("xd", [P, R, F])
            edge_terms = buf("edge_terms", [P, R, 2, 4 * C])
            same = buf("same", [P, 4, P])
            xdT = buf("xdT", [P, 4, F])
            raw = buf("raw", [P, 2, H])
            score = buf("score", [P, 2, H])
            ahead = buf("ahead", [H, 2, P])
            top = buf("top", [H, 2, P])
            below = buf("below", [H, 2, P])
            weightT = buf("weightT", [H, 2, P])
            wmd = buf("wmd", [P, 4, 3 * H])
            rden = buf("rden", [P, 2, H])
            alpha = buf("alpha", [P, 2, H])
            y = buf("y", [P, 2, F])
            aggT = buf("aggT", [P, 4, F])
            res2 = buf("res2", [P, R, F])
            junk2 = buf("junk2", [P, 2, F])
            part2 = buf("part2", [P, R, 1])
            negmean2 = buf("negmean2", [P, R, 1])
            ssq2 = buf("ssq2", [P, R, 1])
            var2 = buf("var2", [P, R, 1])
            rstd2 = buf("rstd2", [P, R, 1])

            proj = psum[:, 0:F]
            turned = psum[:, 2 * 512:2 * 512 + F]
            zT = psum[:, 4 * 512:4 * 512 + F]
            scoreT_ps = psum[0:H, 7 * 512:7 * 512 + P]
            wm_ps = psum[:, 7 * 512 + P:7 * 512 + P + 2 * H]
            den_ps = psum[:, 7 * 512 + P + 2 * H:7 * 512 + P + 3 * H]

            def sems(names):
                return [sem(n) for n in names.split()]

            cleared = sem("cleared")
            rows_in, apart_in, xs_in, xd_in, terms_in, out_done = ([sem(f"{n}{s}") for s in range(R)] for n in
                ("rows_in", "apart_in", "xs_in", "xd_in", "terms_in", "out_done"))
            terms_out = [sem(f"terms_out{q}") for q in range(4)]
            (idx_set, out_idx_set, rstd_set) = sems("idx_set out_idx_set rstd_set")
            (wm_done, z_done, den_done, xd_turned, scoreT_done, sums_turned, proj_done) = sems(
                "wm_done z_done den_done xd_turned scoreT_done sums_turned proj_done")
            (ssq_set, xdT_set, aggT_set, exp_done, sums_taken) = sems("ssq_set xdT_set aggT_set exp_done sums_taken")
            (wm_set, raw_set, score_set, res_set, mean_set, rden_set, alpha_set, den_set, y_set, ahead_set, top_set,
             below_set, same_set, var_set, norm_set, passed_set) = sems(
                "wm_set raw_set score_set res_set mean_set rden_set alpha_set den_set y_set ahead_set top_set "
                "below_set same_set var_set norm_set passed_set")

            class Blk:
                def __init__(self, lap, s):
                    self.lap, self.s = lap + s // R, s % R
                    self.n = self.s + R * self.lap
                    static = isinstance(self.n, int)
                    self.level = max(k for k, f in enumerate(FIRST) if f <= self.n) if static and self.n >= 0 else 0
                    self.j = self.n - FIRST[self.level]
                    self.i, self.q = self.s % 2, self.s % 4
                    self.uses = 16 * (self.lap + 1)

                def quarter_uses(self):
                    return 32 * self.lap + 16 * (self.s // 4 + 1)

                def pick(self, w=1):
                    return bass.ds(self.n, w) if not isinstance(self.n, int) else slice(self.n, self.n + w)

            AHEAD, BEHIND, BEHIND_NEEDED = 7, 6, 4

            def needs(level, j):
                return FIRST[level - 1] + min((j + 1) * (P // 2), LEVELS[level - 1]) - 1

            at_step = {n: n for n in range(LEVELS[0])}
            for k in range(1, len(LEVELS)):
                start = max([at_step[FIRST[k] - 1] + 1] +
                            [at_step[needs(k, j)] + BEHIND_NEEDED - j for j in range(LEVELS[k])])
                at_step.update({FIRST[k] + j: start + j for j in range(LEVELS[k])})
            block_of = {p: n for n, p in at_step.items()}
            assert all(at_step[n + 1] == at_step[n] + 1 for n in range(0, NBLK - 1, 2))

            def walk(eng, step):
                def at(p):
                    return lambda k=0: Blk(0, block_of[p + k]) if p + k in block_of else None

                def in_lap(lap, s):
                    return lambda k=0: Blk(lap, s + k)
                first = 2
                last = max(first, (LEVELS[0] - AHEAD) // R)
                for p in range(-AHEAD, R * first):
                    step(at(p))
                if last > first:
                    with eng.Fori(first, last) as lap:
                        for s in range(R):
                            step(in_lap(lap, s))
                for p in range(R * last, max(block_of) + BEHIND + 1):
                    step(at(p))

            with nc.Block() as block:
                @block.sync
                def _(sp):
                    def step(blk):
                        if b := blk(4):
                            hold(sp, same_set, b.n - R + 1)
                            hold(sp, top_set, b.n - R + 1)
                            sp.dma_start(dst_row[:, b.s, :], rows[b.pick(), 0:P].to_broadcast([P, P])
                                         ).then_inc(rows_in[b.s], 16)
                            sp.dma_start(apart[:, b.s, 1:P + 1], apart_rows[b.pick(), :].to_broadcast([H, P])
                                         ).then_inc(apart_in[b.s], 16)
                        if (b := blk()) and b.level < len(LEVELS) - 1:
                            to = (slice(2 * b.j, 2 * b.j + 2) if isinstance(b.j, int) else bass.ds(2 * b.j, 2))
                            hold(sp, den_set, b.n + 1)
                            sp.dma_start(passed_terms[b.level][to, :], wmd[0:P:P - 1, b.q, H:3 * H]
                                         ).then_inc(terms_out[b.q], 16)
                    walk(sp, step)

                @block.gpsimd
                def _(pool):
                    nc.gpsimd.memset(apart[:, :, 0:1], 0.0).then_inc(cleared, 1)
                    nc.gpsimd.memset(edge_terms[:], 0.0).then_inc(cleared, 1)
                    if LEVELS[0] <= R:
                        nc.gpsimd.memset(xd[:], 0.0).then_inc(cleared, 1)
                        nc.gpsimd.memset(xs[:], 0.0).then_inc(cleared, 1)
                    pool.wait_ge(cleared, 4 if LEVELS[0] <= R else 2)

                    def gather(b, dest, source, k, done):
                        nc.gpsimd.indirect_dma_start(
                            out=dest, out_offset=None, in_=source,
                            in_offset=bass.IndirectOffsetOnAxis(ap=idx[:, b.s, k:k + 1], axis=0),
                            bounds_check=N - 1, oob_is_err=False).then_inc(done[b.s], 16)

                    def take(b):
                        for q in range(4):
                            pool.wait_ge(terms_out[q], 16 * len(range(q, needs(b.level, b.j) + 1, 4)))
                        e0, e1 = b.j * P, min((b.j + 1) * P, 2 * LEVELS[b.level - 1])
                        pool.dma_start(edge_terms[0:e1 - e0, b.s, 0, :], passed_terms[b.level - 1][e0:e1, :]
                                       ).then_inc(terms_in[b.s], 32)

                    def step(blk):
                        if b := blk(5):
                            hold(pool, idx_set, b.n + 1)
                            hold(pool, res_set, b.n + 1 - R)
                            gather(b, xd[:, b.s, :], x, 1, xd_in)
                            if not b.level:
                                gather(b, edge_terms[:, b.s, 1, :], table, 1, terms_in)
                                gather(b, edge_terms[:, b.s, 0, :], table, 0, terms_in)
                            else:
                                take(b)
                        if (b := blk(4)) and not b.level:
                            gather(b, xs[:, b.s, :], x, 0, xs_in)
                        if (b := blk(-4)) and b.s % 2 == 0:
                            w = 2 if blk(-3) else 1
                            hold(pool, var_set, b.n + w)
                            nc.gpsimd.tensor_tensor(rstd2[:, b.s:b.s + w, 0], var2[:, b.s:b.s + w, 0],
                                                    half[:].to_broadcast([P, w]), ALU.pow).then_inc(rstd_set, w)
                        if b := blk(-6):
                            hold(pool, out_idx_set, b.n + 1)
                            hold(pool, norm_set, b.n + 1)
                            nc.gpsimd.indirect_dma_start(
                                out=out, out_offset=bass.IndirectOffsetOnAxis(ap=out_idx[:, b.s:b.s + 1], axis=0),
                                in_=res2[:, b.s, :], in_offset=None,
                                bounds_check=N - 1, oob_is_err=False).then_inc(out_done[b.s], 16)
                    walk(pool, step)
                    for s in range(R):
                        pool.wait_ge(out_done[s], 16 * len(range(s, NBLK, R)))

                @block.tensor
                def _(pe):
                    def step(blk):
                        if b := blk():
                            pe.wait_ge(y_set, b.n + 1)
                            wait(pe, aggT_set, b.n)
                            for c in range(C):
                                last = nc.tensor.matmul(zT[:, c * P:(c + 1) * P], y[:, b.i, c * P:(c + 1) * P],
                                                        same[:, b.q, :], start=True, stop=True)
                            last.then_inc(z_done, 1)
                        if b := blk(1):
                            hold(pe, exp_done, b.n + 1)
                            hold(pe, below_set, b.n + 1)
                            nc.tensor.transpose(wm_ps[:, 0:H], weightT[:, b.i, :], ident[0:H, 0:H])
                            nc.tensor.transpose(wm_ps[:, H:2 * H], top[:, b.i, :], ident[0:H, 0:H]
                                                ).then_inc(wm_done, 1)
                        if b := blk(3):
                            pe.wait_ge(xd_in[b.s], b.uses)
                            wait(pe, xdT_set, b.n)
                            if b.level:
                                wait(pe, sums_taken, b.n - LEVELS[0])
                            for c in range(C):
                                last = nc.tensor.transpose(turned[:, c * P:(c + 1) * P],
                                                           xd[:, b.s, c * P:(c + 1) * P], ident[:])
                            last.then_inc(xd_turned, 1)
                            if b.level:
                                pe.wait_ge(passed_set, needs(b.level, b.j) + 1)
                                pe.wait_ge(xdT_set, b.n + 1)
                                e0, e1 = b.j * P, min((b.j + 1) * P, 2 * LEVELS[b.level - 1])
                                for c in range(C):
                                    last = nc.tensor.transpose(turned[0:e1 - e0, c * P:(c + 1) * P],
                                                               passed_sums[b.level - 1][:, c, e0:e1], ident[:])
                                last.then_inc(sums_turned, 1)
                        if b := blk(1):
                            pe.wait_ge(wm_set, b.n + 1)
                            pe.wait_ge(same_set, b.n + 1)
                            nc.tensor.matmul(den_ps, same[:, b.q, :], wmd[:, b.q, 0:H], start=True, stop=True
                                             ).then_inc(den_done, 1)
                        if b := blk():
                            wait(pe, res_set, b.n)
                            for c in range(C):
                                nc.tensor.matmul(proj[:, c * P:(c + 1) * P], xdT[:, b.q, c * P:(c + 1) * P],
                                                 w_node[:, c, 0:P], start=(c % 4 == 0), stop=False)
                        if b := blk(2):
                            pe.wait_ge(score_set, b.n + 1)
                            wait(pe, den_set, b.n)
                            nc.tensor.transpose(scoreT_ps, score[:, b.i, :], ident[:]).then_inc(scoreT_done, 1)
                        if b := blk():
                            pe.wait_ge(aggT_set, b.n + 1)
                            for c in range(C):
                                last = nc.tensor.matmul(proj[:, c * P:(c + 1) * P], aggT[:, b.q, c * P:(c + 1) * P],
                                                        w_agg[:], start=False, stop=(c in (3, C - 1)))
                            last.then_inc(proj_done, 1)
                    walk(pe, step)

                @block.scalar
                def _(act):
                    def step(blk):
                        if b := blk():
                            act.wait_ge(z_done, b.n + 1)
                            wait(act, proj_done, b.n - 3)
                            wait(act, passed_set, b.n - 3)
                            nc.scalar.copy(aggT[:, b.q, :], zT).then_inc(aggT_set, 1)
                        if b := blk(3):
                            act.wait_ge(xd_turned, b.n + 1)
                            wait(act, proj_done, b.n - 3)
                            nc.scalar.copy(xdT[:, b.q, :], turned).then_inc(xdT_set, 1)
                            if b.level:
                                e = min(P, 2 * LEVELS[b.level - 1] - b.j * P)
                                act.wait_ge(sums_turned, b.n + 1 - LEVELS[0])
                                wait(act, y_set, b.n - R + 1)
                                nc.scalar.copy(xs[0:e, b.s, :], turned[0:e, :]).then_inc(sums_taken, 1)
                        if b := blk(-1):
                            act.wait_ge(mean_set, b.n + 1)
                            wait(act, ssq_set, b.n - 1)
                            nc.scalar.activation(junk2[:, b.i, :], res2[:, b.s, :], ACT.Square,
                                                 bias=negmean2[:, b.s, :], accum_out=ssq2[:, b.s, :]
                                                 ).then_inc(ssq_set, 1)
                        if b := blk(2):
                            act.wait_ge(below_set, b.n + 1)
                            wait(act, wm_done, b.n - 1)
                            nc.scalar.activation(weightT[:, b.i, :], below[:, b.i, :], ACT.Exp).then_inc(exp_done, 1)
                    walk(act, step)

                @block.vector
                def _(dve):
                    dve.wait_ge(cleared, 4 if LEVELS[0] <= R else 2)

                    def step(blk):
                        if b := blk(-1):
                            dve.wait_ge(proj_done, b.n + 1)
                            wait(dve, out_done[b.s], b.uses - 16)
                            nc.vector.scalar_tensor_tensor(out=res2[:, b.s, :], in0=proj, scalar=0.0,
                                                           in1=xd[:, b.s, :], op0=ALU.max, op1=ALU.add,
                                                           accum_out=part2[:, b.s, :]).then_inc(res_set, 1)
                        if (b := blk(-1)) and b.level < len(LEVELS) - 1:
                            dve.wait_ge(aggT_set, b.n + 1)
                            to = (slice(2 * b.j, 2 * b.j + 2) if isinstance(b.j, int) else bass.ds(2 * b.j, 2))
                            nc.vector.tensor_copy(
                                passed_sums[b.level][:, :, to],
                                aggT[:, b.q, :].rearrange("p (c w) -> p c w", c=C)[:, :, 0:P:P - 1]
                                ).then_inc(passed_set, 1)
                        if b := blk(2):
                            dve.wait_ge(terms_in[b.s], 2 * b.uses)
                            wait(dve, score_set, b.n - 1)
                            if not b.level:
                                nc.vector.tensor_tensor(
                                    raw[:, b.i, :].rearrange("p (c m) -> p c m", m=2),
                                    edge_terms[:, b.s, 1, :].rearrange("p (c w) -> p c w", w=4)[:, :, 0:2],
                                    edge_terms[:, b.s, 0, :].rearrange("p (c w) -> p c w", w=4)[:, :, 2:4],
                                    ALU.add).then_inc(raw_set, 1)
                                dve.wait_ge(raw_set, b.n + 1)
                                wait(dve, scoreT_done, b.n - 1)
                                nc.vector.scalar_tensor_tensor(out=score[:, b.i, :], in0=raw[:, b.i, :], scalar=SLOPE,
                                                               in1=raw[:, b.i, :], op0=ALU.mult, op1=ALU.max
                                                               ).then_inc(score_set, 1)
                            else:
                                wait(dve, scoreT_done, b.n - 1)
                                nc.vector.tensor_copy(score[:, b.i, :], edge_terms[:, b.s, 0, 0:H]).then_inc(score_set, 1)
                        if b := blk(1):
                            dve.wait_ge(wm_done, b.n + 1)
                            if b.level < len(LEVELS) - 1:
                                wait(dve, terms_out[b.q], b.quarter_uses() - 16)
                            wait(dve, alpha_set, b.n - 3)
                            if not b.level:
                                nc.vector.tensor_copy(wmd[:, b.q, 0:2 * H], wm_ps).then_inc(wm_set, 1)
                            else:
                                nc.vector.tensor_copy(wmd[:, b.q, H:2 * H], wm_ps[:, H:2 * H])
                                nc.vector.tensor_tensor(wmd[:, b.q, 0:H], wm_ps[:, 0:H],
                                                        edge_terms[:, b.s, 0, H:2 * H], ALU.mult).then_inc(wm_set, 1)
                        if b := blk(-1):
                            dve.wait_ge(res_set, b.n + 1)
                            nc.vector.tensor_scalar(negmean2[:, b.s, :], part2[:, b.s, :], -1.0 / F, None, ALU.mult
                                                    ).then_inc(mean_set, 1)
                        if (b := blk(6)) and b.s % 2 == 0:
                            w = 2 if blk(7) else 1
                            nc.vector.tensor_copy(idx[:, b.s:b.s + w, :], all_cols[:, b.pick(w), :]
                                                  ).then_inc(idx_set, w)
                        if (b := blk(-5)) and b.s % 2 == 0:
                            w = 2 if blk(-4) else 1
                            nc.vector.tensor_copy(out_idx[:, b.s:b.s + w], all_cols[:, b.pick(w), 2]
                                                  ).then_inc(out_idx_set, w)
                        if b := blk(-5):
                            dve.wait_ge(rstd_set, b.n + 1)
                            nc.vector.tensor_scalar(res2[:, b.s, :], res2[:, b.s, :], negmean2[:, b.s, :],
                                                    rstd2[:, b.s, :], ALU.add, ALU.mult).then_inc(norm_set, 1)
                        if b := blk(1):
                            dve.wait_ge(den_done, b.n + 1)
                            wait(dve, alpha_set, b.n - 1)
                            nc.vector.reciprocal(rden[:, b.i, :], den_ps).then_inc(rden_set, 1)
                            nc.vector.tensor_scalar(wmd[:, b.q, 2 * H:3 * H], den_ps, idx[:, b.s, 3:4], None, ALU.mult
                                                    ).then_inc(den_set, 1)
                        if b := blk(1):
                            dve.wait_ge(rden_set, b.n + 1)
                            wait(dve, y_set, b.n - 1)
                            nc.vector.tensor_tensor(alpha[:, b.i, :], wmd[:, b.q, 0:H], rden[:, b.i, :], ALU.mult
                                                    ).then_inc(alpha_set, 1)
                            dve.wait_ge(alpha_set, b.n + 1)
                            if not b.level:
                                dve.wait_ge(xs_in[b.s], b.uses)
                            else:
                                dve.wait_ge(sums_taken, b.n + 1 - LEVELS[0])
                            wait(dve, z_done, b.n - 1)
                            nc.vector.tensor_tensor(
                                y[:, b.i, :].rearrange("p (h d) -> p h d", d=D),
                                xs[:, b.s, :].rearrange("p (h d) -> p h d", d=D),
                                alpha[:, b.i, :].unsqueeze(2).to_broadcast([P, H, D]), ALU.mult).then_inc(y_set, 1)
                        if (b := blk(-3)) and b.s % 2 == 0:
                            w = 2 if blk(-2) else 1
                            dve.wait_ge(ssq_set, b.n + w)
                            nc.vector.tensor_scalar(var2[:, b.s:b.s + w, :], ssq2[:, b.s:b.s + w, :], 1.0 / F, EPS,
                                                    ALU.mult, ALU.add).then_inc(var_set, w)
                        if b := blk(2):
                            dve.wait_ge(scoreT_done, b.n + 1)
                            dve.wait_ge(apart_in[b.s], b.uses)
                            wait(dve, top_set, b.n - 1)
                            nc.vector.tensor_tensor_scan(ahead[:, b.i, :], apart[:, b.s, 0:P], scoreT_ps,
                                                         LOWEST, ALU.add, ALU.max).then_inc(ahead_set, 1)
                            dve.wait_ge(ahead_set, b.n + 1)
                            wait(dve, wm_done, b.n - 1)
                            nc.vector.tensor_tensor_scan(top[:, b.i, ::-1], apart[:, b.s, P:0:-1],
                                                         ahead[:, b.i, ::-1], LOWEST, ALU.add, ALU.max
                                                         ).then_inc(top_set, 1)
                            dve.wait_ge(top_set, b.n + 1)
                            wait(dve, exp_done, b.n - 1)
                            nc.vector.tensor_tensor(below[:, b.i, :], scoreT_ps, top[:, b.i, :], ALU.subtract
                                                    ).then_inc(below_set, 1)
                            dve.wait_ge(rows_in[b.s], b.uses)
                            dve.wait_ge(idx_set, b.n + 1)
                            wait(dve, z_done, b.n - 3)
                            nc.vector.tensor_scalar(same[:, b.q, :], dst_row[:, b.s, :], idx[:, b.s, 1:2], None,
                                                    ALU.is_equal).then_inc(same_set, 1)
                    walk(dve, step)

_INS = ['x', 'L0_gnn_W_fc', 'L0_gnn_attn_l', 'L0_gnn_attn_r', 'L0_gnn_W_res']


def kernel(**inputs):
    import numpy as _np
    import concourse.bacc as _bacc
    from concourse import mybir as _mybir
    from concourse.bass_utils import run_bass_kernel_spmd as _run

    x = _np.ascontiguousarray(inputs['x'])
    src, dst = _np.asarray(inputs['src']), _np.asarray(inputs['dst'])
    n, e = x.shape[0], src.shape[0]
    cols, rows, levels = [], [], []
    srcs, dsts = src, dst
    while True:
        m = -(-dsts.shape[0] // P)
        pad = _np.full((m * P + 1 - dsts.shape[0],), n, dst.dtype)
        ds = _np.concatenate([dsts, pad])
        ss = _np.concatenate([srcs, pad])
        d2 = ds[:-1].reshape(m, P)
        ends = [_np.broadcast_to(d2[:, k:k + 1], (m, P)) for k in (0, P - 1)]
        if m == 1:
            ends = [_np.full((m, P), -1, dst.dtype)] * 2
        cols.append(_np.stack([ss[:-1].reshape(m, P), d2, ds[1:].reshape(m, P), *ends], axis=-1))
        rows.append(_np.concatenate([d2, ds[P::P].reshape(m, 1)], axis=1))
        levels.append(m)
        if m == 1:
            break
        dsts = d2[:, [0, P - 1]].reshape(-1)
        srcs = _np.full(dsts.shape, n, src.dtype)
    cols = _np.concatenate(cols).transpose(1, 0, 2)
    rows = _np.concatenate(rows)

    nc = _bacc.Bacc("TRN2", target_bir_lowering=False, num_devices=1)
    named = {k: _np.ascontiguousarray(inputs[k]) for k in _INS}
    named['edge_cols'], named['dst_rows'] = _np.ascontiguousarray(cols), _np.ascontiguousarray(rows)
    arrays, args = {}, []
    for name, a in named.items():
        arrays[f"in_{name}_dram"] = a
        args.append(nc.dram_tensor(f"in_{name}_dram", a.shape, _mybir.dt.from_np(a.dtype), kind="ExternalInput").ap())
    args.append(nc.dram_tensor("out_0_dram", x.shape, _mybir.dt.float32, kind="ExternalOutput").ap())
    gnn_program(nc, *args, levels)
    r = _run(nc, [arrays], core_ids=[0])
    return r.results[0]["out_0_dram"]
```
